# Optimizing a Trainium2 kernel written in Bass

```python
import numpy as np
import jax
import jax.numpy as jnp

def _softmax(x, axis=-1):
    return jax.nn.softmax(x, axis=axis)

def _gelu(x):
    return jax.nn.gelu(x, approximate=True)

def _silu(x):
    return jax.nn.silu(x)

def _sigmoid(x):
    return jax.nn.sigmoid(x)

def _layernorm(x, axis=-1, eps=1e-05):
    m = jnp.mean(x, axis=axis, keepdims=True)
    v = jnp.var(x, axis=axis, keepdims=True)
    return (x - m) / jnp.sqrt(v + eps)

def _scatter_add(tgt, idx, src, axis=0):
    return tgt.at[idx].add(src)

def _segment_sum(src, seg, n):
    return jax.ops.segment_sum(src, seg, n)
kernel_name = 'mk_flamingo_gated_d1_seqx_r8_921037'

def setup_inputs(seed: int=0):
    np.random.seed(seed)
    _w = jnp.asarray

    def _rec_inputs():
        import jax
        import jax.numpy as jnp
        _rk = jax.random.key(seed)
        x = 0.01048 + 0.1018 * jax.random.normal(jax.random.fold_in(_rk, 1), (4, 256, 256), jnp.float32)
        _lenS = 256 - jax.random.randint(jax.random.fold_in(_rk, 7), (4,), 0, max(1, 256 // 4) + 1, jnp.int32)
        _lenS2 = 256 - jax.random.randint(jax.random.fold_in(_rk, 8), (4,), 0, max(1, 256 // 4) + 1, jnp.int32)
        _ctx_512P = jax.random.normal(jax.random.fold_in(_rk, 11), (4, 16, 64), jnp.float32)
        _ctx_512c = jax.random.dirichlet(jax.random.fold_in(_rk, 511), 0.3 * jnp.ones((16,), jnp.float32), (4, 256))
        _ctx_512t = jnp.einsum('bsk,bkd->bsd', _ctx_512c, _ctx_512P)
        _ctx_512t = _ctx_512t * jax.lax.rsqrt(jnp.mean(jnp.square(_ctx_512t)) + 1e-12) * 0.953939
        ctx_512 = -0.000292821 + 1.00034 * (_ctx_512t + 0.3 * jax.random.normal(jax.random.fold_in(_rk, 611), (4, 256, 64), jnp.float32))
        _g = jax.random.normal(jax.random.fold_in(_rk, 9001), (2, 1), jnp.float32)
        _g = jnp.sign(_g) * jnp.maximum(jnp.abs(_g), 1.0) + (_g == 0) * 1.0
        g_xattn = _g[0]
        g_ffn = _g[1]
        return (x, ctx_512, g_xattn, g_ffn)
    x, ctx_512, g_xattn, g_ffn = _rec_inputs()

    def _L0_xattn_setup():
        import jax, jax.numpy as jnp
        import numpy as np
        LRELU_ALPHA = 0.2
        MASK_VAL = -10000000000.0
        B, N, F_IN = (4, 256, 64)
        H, F_OUT = (8, 32)
        F_HID = H * F_OUT

        def gat_layer(x, adj, W, a_self, a_neigh, b):
            feat = jnp.einsum('nf,hfo->hno', x, W)
            attn_self = jnp.einsum('hno,ho->hn', feat, a_self)
            attn_neigh = jnp.einsum('hno,ho->hn', feat, a_neigh)
            e = attn_self[:, :, None] + attn_neigh[:, None, :]
            e = jax.nn.leaky_relu(e, LRELU_ALPHA)
            e = e + MASK_VAL * (1.0 - adj)[None, :, :]
            alpha = jax.nn.softmax(e, axis=-1)
            out = jnp.einsum('hnm,hmo->hno', alpha, feat) + b[:, None, :]
            out = jnp.transpose(out, (1, 0, 2)).reshape(out.shape[1], -1)
            return jax.nn.elu(out)
        key = jax.random.key(seed)
        ks = jax.random.split(key, 10)
        feats = jax.random.normal(ks[0], (B, N, F_IN), dtype=jnp.float32)
        a = (jax.random.uniform(ks[1], (B, N, N)) < 0.01).astype(jnp.float32)
        adj = jnp.maximum(a, jnp.eye(N, dtype=jnp.float32)[None])
        s0 = 1.0 / np.sqrt(F_IN)
        s1 = 1.0 / np.sqrt(F_HID)
        return {'feats': feats, 'adj': adj, 'W0': jax.random.normal(ks[2], (H, F_IN, F_OUT), dtype=jnp.float32) * s0, 'a_self0': jax.random.normal(ks[3], (H, F_OUT), dtype=jnp.float32) * 0.1, 'a_neigh0': jax.random.normal(ks[4], (H, F_OUT), dtype=jnp.float32) * 0.1, 'b0': jnp.zeros((H, F_OUT), dtype=jnp.float32), 'W1': jax.random.normal(ks[5], (H, F_HID, F_OUT), dtype=jnp.float32) * s1, 'a_self1': jax.random.normal(ks[6], (H, F_OUT), dtype=jnp.float32) * 0.1, 'a_neigh1': jax.random.normal(ks[7], (H, F_OUT), dtype=jnp.float32) * 0.1, 'b1': jnp.zeros((H, F_OUT), dtype=jnp.float32)}
    _L0_xattn_all = _L0_xattn_setup()
    _L0_xattn_in = {k: v for k, v in _L0_xattn_all.items() if k in ('W0', 'a_self0', 'a_neigh0', 'b0', 'W1', 'a_self1', 'a_neigh1', 'b1')}
    del _L0_xattn_all

    def _L0_ffn_setup():
        import jax, jax.numpy as jnp
        import numpy as np
        DIM = 256
        EXPERT_DIM = 128
        N_EXPERTS = 16
        TOPK = 2
        N_SHARED = 1
        B, T = (4, 256)
        key = jax.random.key(seed)
        ks = jax.random.split(key, 9)
        s = 0.02
        return {'x': jax.random.normal(ks[0], (B, T, DIM), jnp.float32), 'router_w': jax.random.normal(ks[1], (N_EXPERTS, DIM), jnp.float32) * s, 'router_bias': jnp.zeros((N_EXPERTS,), jnp.float32), 'Wu': jax.random.normal(ks[2], (N_EXPERTS, DIM, EXPERT_DIM), jnp.float32) * s, 'Wg': jax.random.normal(ks[3], (N_EXPERTS, DIM, EXPERT_DIM), jnp.float32) * s, 'Wd': jax.random.normal(ks[4], (N_EXPERTS, EXPERT_DIM, DIM), jnp.float32) * s, 'Su': jax.random.normal(ks[5], (N_SHARED, DIM, EXPERT_DIM * TOPK), jnp.float32) * s, 'Sg': jax.random.normal(ks[6], (N_SHARED, DIM, EXPERT_DIM * TOPK), jnp.float32) * s, 'Sd': jax.random.normal(ks[7], (N_SHARED, EXPERT_DIM * TOPK, DIM), jnp.float32) * s}
    _L0_ffn_all = _L0_ffn_setup()
    _L0_ffn_in = {k: v for k, v in _L0_ffn_all.items() if k in ('router_w', 'router_bias', 'Wu', 'Wg', 'Wd', 'Su', 'Sg', 'Sd')}
    del _L0_ffn_all
    return {'x': x, 'ctx_512': ctx_512, 'g_xattn': g_xattn, 'g_ffn': g_ffn, 'L0_xattn_W0': _L0_xattn_in['W0'], 'L0_xattn_a_self0': _L0_xattn_in['a_self0'], 'L0_xattn_a_neigh0': _L0_xattn_in['a_neigh0'], 'L0_xattn_b0': _L0_xattn_in['b0'], 'L0_xattn_W1': _L0_xattn_in['W1'], 'L0_xattn_a_self1': _L0_xattn_in['a_self1'], 'L0_xattn_a_neigh1': _L0_xattn_in['a_neigh1'], 'L0_xattn_b1': _L0_xattn_in['b1'], 'L0_ffn_router_w': _L0_ffn_in['router_w'], 'L0_ffn_router_bias': _L0_ffn_in['router_bias'], 'L0_ffn_Wu': _L0_ffn_in['Wu'], 'L0_ffn_Wg': _L0_ffn_in['Wg'], 'L0_ffn_Wd': _L0_ffn_in['Wd'], 'L0_ffn_Su': _L0_ffn_in['Su'], 'L0_ffn_Sg': _L0_ffn_in['Sg'], 'L0_ffn_Sd': _L0_ffn_in['Sd']}

def reference(x, ctx_512, g_xattn, g_ffn, L0_xattn_W0, L0_xattn_a_self0, L0_xattn_a_neigh0, L0_xattn_b0, L0_xattn_W1, L0_xattn_a_self1, L0_xattn_a_neigh1, L0_xattn_b1, L0_ffn_router_w, L0_ffn_router_bias, L0_ffn_Wu, L0_ffn_Wg, L0_ffn_Wd, L0_ffn_Su, L0_ffn_Sg, L0_ffn_Sd):
    import jax
    import jax.numpy as jnp

    def _L0_xattn_ref(feats, adj, W0, a_self0, a_neigh0, b0, W1, a_self1, a_neigh1, b1):
        import jax, jax.numpy as jnp
        import numpy as np
        LRELU_ALPHA = 0.2
        MASK_VAL = -10000000000.0
        B, N, F_IN = (4, 256, 64)
        H, F_OUT = (8, 32)
        F_HID = H * F_OUT

        def gat_layer(x, adj, W, a_self, a_neigh, b):
            feat = jnp.einsum('nf,hfo->hno', x, W)
            attn_self = jnp.einsum('hno,ho->hn', feat, a_self)
            attn_neigh = jnp.einsum('hno,ho->hn', feat, a_neigh)
            e = attn_self[:, :, None] + attn_neigh[:, None, :]
            e = jax.nn.leaky_relu(e, LRELU_ALPHA)
            e = e + MASK_VAL * (1.0 - adj)[None, :, :]
            alpha = jax.nn.softmax(e, axis=-1)
            out = jnp.einsum('hnm,hmo->hno', alpha, feat) + b[:, None, :]
            out = jnp.transpose(out, (1, 0, 2)).reshape(out.shape[1], -1)
            return jax.nn.elu(out)

        def per_graph(x, a):
            h = gat_layer(x, a, W0, a_self0, a_neigh0, b0)
            return gat_layer(h, a, W1, a_self1, a_neigh1, b1)
        return jax.vmap(per_graph)(feats, adj)

    def _L0_ffn_ref(x, router_w, router_bias, Wu, Wg, Wd, Su, Sg, Sd):
        import jax, jax.numpy as jnp
        import numpy as np
        DIM = 256
        EXPERT_DIM = 128
        N_EXPERTS = 16
        TOPK = 2
        N_SHARED = 1
        B, T = (4, 256)
        Bx, Tx, D = x.shape
        flat = x.reshape(Bx * Tx, D)
        logits = flat @ router_w.T
        scores = jax.nn.softmax(logits, axis=-1)
        _, topk_idx = jax.lax.top_k(logits + router_bias, TOPK)
        topk_scores = jnp.take_along_axis(scores, topk_idx, axis=-1)
        topk_scores = topk_scores / topk_scores.sum(-1, keepdims=True)
        combine = jnp.einsum('nk,nke->ne', topk_scores, jax.nn.one_hot(topk_idx, N_EXPERTS, dtype=scores.dtype))
        out = jnp.zeros_like(flat)
        for e in range(N_EXPERTS):
            h = jax.nn.silu(flat @ Wu[e]) * (flat @ Wg[e])
            out = out + combine[:, e:e + 1] * (h @ Wd[e])
        for s in range(N_SHARED):
            out = out + jax.nn.silu(flat @ Su[s]) * (flat @ Sg[s]) @ Sd[s]
        return out.reshape(Bx, Tx, D)
    x = x + jnp.tanh(g_xattn[0]) * _L0_xattn_ref(ctx_512, _layernorm(x, axis=-1), L0_xattn_W0, L0_xattn_a_self0, L0_xattn_a_neigh0, L0_xattn_b0, L0_xattn_W1, L0_xattn_a_self1, L0_xattn_a_neigh1, L0_xattn_b1)
    x = x + jnp.tanh(g_ffn[0]) * _L0_ffn_ref(_layernorm(x, axis=-1), L0_ffn_router_w, L0_ffn_router_bias, L0_ffn_Wu, L0_ffn_Wg, L0_ffn_Wd, L0_ffn_Su, L0_ffn_Sg, L0_ffn_Sd)
    return x

_drawn_inputs = setup_inputs


def setup_inputs(seed=0):
    import zlib

    import numpy as np

    out = dict(_drawn_inputs(seed))
    spreads = {'L0_xattn_b0': (0.0, 0.1), 'L0_xattn_b1': (0.0, 0.1), 'L0_ffn_router_bias': (0.0, 0.8)}
    factors = {'L0_ffn_router_w': 3.919, 'L0_ffn_Wu': 3.734, 'L0_ffn_Wg': 3.658, 'L0_ffn_Wd': 3.674}
    for name, (base, spread) in spreads.items():
        noise = np.random.default_rng([zlib.crc32(name.encode()), seed]).standard_normal(out[name].shape)
        drawn = base * np.exp(spread * noise) if base else spread * noise
        out[name] = jnp.asarray(drawn.astype(out[name].dtype))
    for name, factor in factors.items():
        out[name] = (out[name] * factor).astype(out[name].dtype)
    return out
```

```python
from contextlib import ExitStack

import concourse.bass as bass
from concourse import mybir

F32 = mybir.dt.float32
F32R = mybir.dt.float32r
U32 = mybir.dt.uint32
ALU = mybir.AluOpType
ACT = mybir.ActivationFunctionType
AX = mybir.AxisListType

P = 128
HEADS, F_OUT = 8, 32
SLOPE = 0.2
MASK_SCALE = 1.0e10
EPS = 1.0e-5
HEADROOM = 40.0
EXPERTS, SHARED = 16, 2
STEPS = EXPERTS + SHARED
UG_BANKS = 3
LAG = 2
LOT = 3
RAW_SLOTS = 12
LO_ROW = 32


def flamingo_block(nc, x, ctx_t, gates, w0, w1, a_self, a_neigh, b0, b1, router_t, router_bias,
                   wu, wg, su, sg, wd, sd, out):
    B, N, D = x.shape
    T = N // P
    C = D // P
    HF = HEADS * F_OUT
    WE = HF + HEADS
    F_IN = ctx_t.shape[1]
    PAIRS = HEADS // 2
    LAYERS = 2

    x_view = x.rearrange("g (t p) d -> g p t d", p=P)
    out_view = out.rearrange("g (t p) d -> g p t d", p=P)

    with ExitStack() as ctx:
        def sb(name, shape, dt=F32):
            return ctx.enter_context(nc.sbuf_tensor(name, shape, dt))

        def psum(name, shape):
            return ctx.enter_context(nc.psum_tensor(name, shape, F32))

        def sem(name):
            return ctx.enter_context(nc.semaphore(name))

        ident = sb("ident", [P, P])
        ones = sb("ones", [HEADS * 2, P])
        sel_f = sb("sel_f", [64, EXPERTS, P])
        sel = sb("sel", [64, EXPERTS, P], F32R)
        expert_id = sb("expert_id", [P, EXPERTS])
        minus_half = sb("minus_half", [P, T])
        w_raw = [sb("w0_raw", [F_IN, 1, HF]), sb("w1_raw", [P, C, HF])]
        w_ext = [sb("w0_ext", [F_IN, 1, WE]), sb("w1_ext", [P, C, WE])]
        w_score = [sb("w0_score", [F_IN, 1, 2 * HEADS]), sb("w1_score", [P, C, 2 * HEADS])]
        w_prod = sb("w_prod", [P, C, HF])
        a_bc = [[sb(f"a{i}_{n}", [P, HF]) for n in ("self", "neigh")] for i in range(LAYERS)]
        b_bc = [sb(f"b{i}_bc", [P, HF]) for i in range(LAYERS)]
        gate_raw = sb("gate_raw", [P, 2])
        gate = sb("gate", [P, 2])
        rt_raw = sb("rt_raw", [P, C, EXPERTS])
        rt_hi = sb("rt_hi", [P, C, EXPERTS], F32R)
        rt_lo = sb("rt_lo", [P, C, EXPERTS], F32R)
        rbias = sb("rbias", [P, EXPERTS])
        up_raw = sb("up_raw", [P, RAW_SLOTS, 2, C * P])
        up_hi = sb("up_hi", [P, STEPS, 2, C * P], F32R)
        up_lo = sb("up_lo", [P, STEPS, 2, C * P], F32R)
        down_w = sb("down_w", [P, STEPS, D])

        x_in = sb("x_in", [P, T, D])
        xc_t = sb("xc_t", [F_IN, 1, N])
        x_less_gate = sb("x_less_gate", [P, T, D])
        stats = sb("stats", [P, T, 6])
        meanvar = sb("meanvar", [P, T, 2])
        var_eps = sb("var_eps", [P, T])
        rstd = sb("rstd", [P, T])
        mask = sb("mask", [P, T, D])
        row_max = sb("row_max", [P, T])
        mask_t = sb("mask_t", [P, C, N])
        score_max = sb("score_max", [2 * HEADS, 1])
        diag = sb("diag", [2 * HEADS, 2 * HEADS])
        self_rows = sb("self_rows", [64, N], F32R)
        max_bc = sb("max_bc", [P, 2 * HEADS])
        shift = sb("shift", [P, HEADS])
        t_nat = sb("t_nat", [P, C, HEADS])
        t_08 = sb("t_08", [P, C, HEADS])
        exp_bias = sb("exp_bias", [P, C, HEADS])
        feat = sb("feat", [P, C, HEADS, F_OUT + 1])
        prob = sb("prob", [P, HEADS, C, N])
        inv_sum = sb("inv_sum", [P, T, HEADS])
        att = sb("att", [P, T, HF])
        att_exp = sb("att_exp", [P, T, HF])
        att_z = sb("att_z", [P, T, HF])
        h1_t = sb("h1_t", [P, C, N])
        x2 = sb("x2", [P, T, D])
        x_hat = sb("x_hat", [P, T, D])

        stage_hi = sb("stage_hi", [P, C, N], F32R)
        stage_lo = sb("stage_lo", [P, C, N], F32R)
        biased = sb("biased", [P, T, EXPERTS])
        top8 = sb("top8", [P, T, 8])
        top_at = sb("top_at", [P, T, 8], U32)
        top_at_f = sb("top_at_f", [P, T, 8])
        logit_max = sb("logit_max", [P, T])
        r_exp = sb("r_exp", [P, T, EXPERTS])
        picked = sb("picked", [P, T, EXPERTS])
        r_sum = sb("r_sum", [P, T])
        r_inv = sb("r_inv", [P, T])
        combine = sb("combine", [P, T, EXPERTS])
        comb_rows = sb("comb_rows", [64, N], F32R)

        x_hi = sb("x_hi", [P, C, N], F32R)
        x_lo = sb("x_lo", [P, C, N], F32R)
        x2_ffn = sb("x2_ffn", [P, T, D])
        th = sb("th", [P, 2, N])
        hid = sb("hid", [P, 2, N])
        hid_out = sb("hid_out", [P, 3, N])
        y_out = sb("y_out", [P, T, D])

        ps_ug = [psum(f"ps_ug{i}", [P, 2, N]) for i in range(UG_BANKS)]
        ps_comb = psum("ps_comb", [P, 2, N])
        ps_acc = psum("ps_acc", [P, T, D])
        ps_row = [psum(f"ps_row{i}", [P, 512]) for i in range(T)]
        ps_mix = psum("ps_mix", [P, 512])
        mix_pair = ps_mix[:, :].rearrange("p (a n) -> p a n", a=2)

        x_landed, ctx_landed = sem("x_landed"), sem("ctx_landed")
        gates_landed = sem("gates_landed")
        gat_landed = [sem(f"gat{i}_landed") for i in range(LAYERS)]
        router_landed = sem("router_landed")
        up_landed = [sem(f"up_landed{i}") for i in range(STEPS // LOT)]
        down_landed = sem("down_landed")
        out_stored = sem("out_stored")
        pool_const, const_ready = sem("pool_const"), sem("const_ready")
        gate_ready, sel_ready, rt_ready = sem("gate_ready"), sem("sel_ready"), sem("rt_ready")
        gat_ready = sem("gat_ready")
        w_steps = sem("w_steps")
        up_hi_ready, up_ready = sem("up_hi_ready"), sem("up_ready")
        dve_att = sem("dve_att")
        var_ready, rstd_ready = sem("var_ready"), sem("rstd_ready")
        xg_ready = sem("xg_ready")
        mask_ready, mask_turned, mask_t_ready = sem("mask_ready"), sem("mask_turned"), sem("mask_t_ready")
        rows_ready, diag_ready, max_spread, max_ready = (sem("rows_ready"), sem("diag_ready"),
                                                         sem("max_spread"), sem("max_ready"))
        feat_ps, feat_ready, bias_ready = sem("feat_ps"), sem("feat_ready"), sem("bias_ready")
        self_spread, relu_done, add_done = sem("self_spread"), sem("relu_done"), sem("add_done")
        exp_done, pv_done, rows_free = sem("exp_done"), sem("pv_done"), sem("rows_free")
        neg_ready, neg_exp, z_ready = sem("neg_ready"), sem("neg_exp"), sem("z_ready")
        z_turned, h1_ready = sem("z_turned"), sem("h1_ready")
        x2_ready = sem("x2_ready")
        xhat_ready, xhat_turned = sem("xhat_ready"), sem("xhat_turned")
        stage_hi_ready, stage_ready = sem("stage_hi_ready"), sem("stage_ready")
        logits_ready, rexp_in, rexp_out = sem("logits_ready"), sem("rexp_in"), sem("rexp_out")
        comb_ready, comb_turned, comb_rows_ready = (sem("comb_ready"), sem("comb_turned"),
                                                    sem("comb_rows_ready"))
        dve_ffn = sem("dve_ffn")
        x_hi_moved, x_lo_moved, x2_moved = sem("x_hi_moved"), sem("x_lo_moved"), sem("x2_moved")
        up_done, comb_spread, tanh_done = sem("up_done"), sem("comb_spread"), sem("tanh_done")
        ug_read, hid_ready, down_done, y_ready = (sem("ug_read"), sem("hid_ready"),
                                                  sem("down_done"), sem("y_ready"))


        MASK, MASK_T = 0, 1
        LAYER_AT = (1, 8)
        NORM_AT = (6, 13)
        HAT_AT, ROUTE_AT, TOP_AT, COMB_AT = 14, 15, 16, 17

        block = ctx.enter_context(nc.Block())

        @block.sync
        def _(sp):
            def load_graph(a):
                if a:
                    sp.wait_ge(xg_ready, a)
                    sp.wait_ge(mask_ready, a)
                sp.dma_start(x_in[:], x_view[a]).then_inc(x_landed, 16)
                if a:
                    sp.wait_ge(feat_ps, LAYERS * (a - 1) + 1)
                sp.dma_start(xc_t[:, 0, :], ctx_t[a]).then_inc(ctx_landed, 16)

            def store(g):
                sp.wait_ge(y_ready, g + 1)
                sp.dma_start(out_view[g], y_out[:]).then_inc(out_stored, 16)

            load_graph(0)
            sp.dma_start(gate_raw[:], gates.partition_broadcast(P)).then_inc(gates_landed, 16)
            for i, (w, b) in enumerate(((w0, b0), (w1, b1))):
                sp.dma_start(w_raw[i][:], w.rearrange("(c p) n -> p c n", p=w_raw[i].shape[0])
                             ).then_inc(gat_landed[i], 16)
                sp.dma_start(a_bc[i][0][:], a_self[i].partition_broadcast(P)).then_inc(gat_landed[i], 16)
                sp.dma_start(a_bc[i][1][:], a_neigh[i].partition_broadcast(P)).then_inc(gat_landed[i], 16)
                sp.dma_start(b_bc[i][:], b.partition_broadcast(P)).then_inc(gat_landed[i], 16)
            sp.dma_start(rt_raw[:], router_t.rearrange("(c p) e -> p c e", p=P)).then_inc(router_landed, 16)
            sp.dma_start(rbias[:], router_bias.partition_broadcast(P)).then_inc(router_landed, 16)
            for n, first in enumerate(range(0, STEPS, LOT)):
                if first >= RAW_SLOTS:
                    sp.wait_ge(up_ready, first - RAW_SLOTS + LOT)
                for k, (routed, shared) in enumerate(((wu, su), (wg, sg))):
                    slot = first % RAW_SLOTS
                    r = max(0, min(LOT, EXPERTS - first))
                    sp.dma_start(up_raw[:, slot:slot + r, k, :], routed[:, first:first + r, :]
                                 ).then_inc(up_landed[n], 16)
                    if r < LOT:
                        sp.dma_start(up_raw[:, slot + r:slot + LOT, k, :], shared).then_inc(up_landed[n], 16)
                if first == 0:
                    sp.dma_start(down_w[:, 0:EXPERTS, :], wd).then_inc(down_landed, 16)
                    sp.dma_start(down_w[:, EXPERTS:STEPS, :], sd).then_inc(down_landed, 16)
            for a in range(1, B):
                load_graph(a)
                if a >= 2:
                    store(a - 2)
            store(B - 2)
            store(B - 1)
            sp.wait_ge(out_stored, 16 * B)

        @block.gpsimd
        def _(pool):
            pool.memset(ident[:], 0.0).then_inc(pool_const, 1)
            pool.memset(sel_f[:], 0.0).then_inc(pool_const, 1)
            pool.memset(ones[:], 1.0).then_inc(const_ready, 1)
            pool.memset(minus_half[:], -0.5).then_inc(const_ready, 1)
            pool.memset(feat[:, :, :, F_OUT:F_OUT + 1], 1.0).then_inc(const_ready, 1)
            pool.memset(self_rows[:].bitcast(F32), 0.0).then_inc(const_ready, 1)
            pool.memset(comb_rows[:].bitcast(F32), 0.0).then_inc(const_ready, 1)
            pool.wait_ge(pool_const, 2)
            pool.affine_select(out=ident[:], in_=ident[:], compare_op=ALU.not_equal, fill=1.0, base=0,
                               pattern=[[-1, P]], channel_multiplier=1).then_inc(const_ready, 1)
            pool.iota(expert_id[:], pattern=[[1, EXPERTS]], base=0, channel_multiplier=0,
                      allow_small_or_imprecise_dtypes=True).then_inc(const_ready, 1)
            for k, off in enumerate((0, LO_ROW)):
                pool.affine_select(out=sel_f[:], in_=sel_f[:], compare_op=ALU.not_equal, fill=1.0,
                                   base=-off, pattern=[[-1, EXPERTS], [0, P]],
                                   channel_multiplier=1).then_inc(pool_const, 1)
                pool.wait_ge(pool_const, 3 + k)
            pool.tensor_copy(sel[:], sel_f[:]).then_inc(sel_ready, 1)

            def rstd_of(n):
                pool.wait_ge(var_ready, n)
                pool.tensor_tensor(rstd[:], var_eps[:], minus_half[:], ALU.pow).then_inc(rstd_ready, 1)

            def less_gate(a):
                pool.wait_ge(x_landed, 16 * (a + 1))
                if a == 0:
                    pool.wait_ge(gate_ready, 1)
                else:
                    pool.wait_ge(x2_ready, a)
                for t in range(T):
                    last = pool.tensor_scalar(x_less_gate[:, t], x_in[:, t], gate[:, 0:1], None,
                                              ALU.subtract)
                last.then_inc(xg_ready, 1)

            def split(e):
                pool.wait_ge(up_landed[e // LOT], 32 if (e // LOT + 1) * LOT <= EXPERTS else 64)
                raw = up_raw[:, e % RAW_SLOTS]
                pool.tensor_copy(up_hi[:, e], raw).then_inc(up_hi_ready, 1)
                pool.wait_ge(up_hi_ready, e + 1)
                pool.tensor_tensor(up_lo[:, e], raw, up_hi[:, e].bitcast(F32),
                                   ALU.subtract).then_inc(up_ready, 1)

            def move_x2(g):
                pool.wait_ge(x2_ready, g + 1)
                if g:
                    pool.wait_ge(y_ready, g)
                pool.tensor_copy(x2_ffn[:], x2[:]).then_inc(x2_moved, 1)

            rstd_of(1)
            less_gate(0)
            for e in range(12):
                split(e)
            rstd_of(2)
            for e in range(12, STEPS):
                split(e)
            for g in range(B):
                if g + 1 < B:
                    rstd_of(2 * g + 3)
                    less_gate(g + 1) if False else None
                move_x2(g)
                if g + 1 < B:
                    less_gate(g + 1)
                    rstd_of(2 * g + 4)

        @block.scalar
        def _(act):
            def evict_mask(a):
                act.wait_ge(mask_turned, a + 1)
                if a:
                    act.wait_ge(add_done, LAYERS * PAIRS * a)
                act.activation(mask_t[:].rearrange("p c n -> p (c n)"), ps_mix[:], ACT.Copy
                               ).then_inc(mask_t_ready, 1)

            def evict_features(a, i):
                n = LAYERS * a + i
                act.wait_ge(feat_ps, n + 1)
                if n:
                    act.wait_ge(pv_done, PAIRS * n)
                    act.wait_ge(bias_ready, n)
                for t in range(T):
                    act.activation(feat[:, t, :, 0:F_OUT],
                                   ps_row[t][:, 0:HF].rearrange("p (h o) -> p h o", h=HEADS), ACT.Copy)
                    last = act.activation(t_nat[:, t, :], ps_row[t][:, HF:WE], ACT.Copy)
                last.then_inc(feat_ready, 1)

            def relu(a, i, p):
                n = LAYERS * a + i
                act.wait_ge(self_spread, PAIRS * n + p + 1)
                act.wait_ge(bias_ready, n + 1)
                if n:
                    act.wait_ge(pv_done, PAIRS * (n - 1) + p + 1)
                for k in range(2):
                    for c in range(C):
                        h = 2 * p + k
                        last = act.activation(prob[:, h, c, :], mix_pair[:, k, :], ACT.Relu,
                                              bias=t_08[:, c, h:h + 1])
                last.then_inc(relu_done, 1)

            def exps(a, i, p):
                n = LAYERS * a + i
                act.wait_ge(add_done, PAIRS * n + p + 1)
                for h in range(2 * p, 2 * p + 2):
                    for c in range(C):
                        last = act.activation(prob[:, h, c, :], prob[:, h, c, :], ACT.Exp,
                                              bias=exp_bias[:, c, h:h + 1])
                last.then_inc(exp_done, 1)

            def elu_exp(a, i):
                act.wait_ge(neg_ready, LAYERS * a + i + 1)
                act.activation(att_exp[:], att_exp[:], ACT.Exp).then_inc(neg_exp, 1)

            def stage_high(a):
                act.wait_ge(xhat_turned, a + 1)
                if a:
                    act.wait_ge(x_hi_moved, a)
                act.activation(stage_hi[:].rearrange("p c n -> p (c n)"), ps_mix[:], ACT.Copy
                               ).then_inc(stage_hi_ready, 1)

            def route_exp(a):
                act.wait_ge(rexp_in, a + 1)
                act.activation(r_exp[:], r_exp[:], ACT.Exp).then_inc(rexp_out, 1)

            def attention(a, s):
                if s == MASK_T:
                    evict_mask(a)
                for i in range(LAYERS):
                    if s == LAYER_AT[i]:
                        evict_features(a, i)
                    p = s - LAYER_AT[i] - 1
                    if 0 <= p < PAIRS:
                        relu(a, i, p)
                    if 0 <= p - 1 < PAIRS:
                        exps(a, i, p - 1)
                    if s == NORM_AT[i]:
                        elu_exp(a, i)
                if s == HAT_AT:
                    stage_high(a)
                if s == TOP_AT:
                    route_exp(a)

            def move_hi(g):
                act.wait_ge(stage_ready, g + 1)
                if g:
                    act.wait_ge(up_done, STEPS * g)
                act.activation(x_hi[:], stage_hi[:].bitcast(F32), ACT.Copy).then_inc(x_hi_moved, 1)

            def gate_tanh(g, e):
                n = STEPS * g + e
                act.wait_ge(up_done, n + 1)
                if e >= 2:
                    act.wait_ge(ug_read, n - 1)
                elif g:
                    act.wait_ge(ug_read, n - 1)
                act.activation(th[:, e % 2], ps_ug[e % UG_BANKS][:, 0, :], ACT.Tanh, scale=0.5
                               ).then_inc(tanh_done, 1)

            act.wait_ge(gates_landed, 16)
            act.activation(gate[:], gate_raw[:], ACT.Tanh).then_inc(gate_ready, 1)
            for s in range(STEPS):
                attention(0, s)
            for g in range(B):
                move_hi(g)
                for e in range(STEPS):
                    gate_tanh(g, e)
                    if g + 1 < B:
                        attention(g + 1, e)

        @block.vector
        def _(dve):
            marks = [0, 0]

            def mark(ins):
                ins.then_inc(dve_att, 1)
                marks[0] += 1

            def settle():
                dve.wait_ge(dve_att, marks[0])

            def link(ins):
                mark(ins)
                settle()

            def gat_weights(i):
                K, c = w_raw[i].shape[0], w_raw[i].shape[1]
                dve.wait_ge(gat_landed[i], 64)
                prod = w_prod[0:K, 0:c, :]
                for k, (a, dst) in enumerate(((a_bc[i][0], w_score[i][:, :, 0:HEADS]),
                                              (a_bc[i][1], w_score[i][:, :, HEADS:2 * HEADS]))):
                    link(dve.tensor_tensor(prod, w_raw[i][:],
                                           a[0:K, :].unsqueeze(1).to_broadcast([K, c, HF]), ALU.mult))
                    link(dve.tensor_reduce(dst, prod.rearrange("p c (h o) -> p c h o", h=HEADS), AX.X, ALU.add))
                mark(dve.tensor_copy(w_ext[i][:, :, HF:WE], w_score[i][:, :, HEADS:2 * HEADS]))
                link(dve.tensor_scalar(w_score[i][:, :, 0:HEADS], w_score[i][:, :, 0:HEADS],
                                       1.0 - SLOPE, None, ALU.mult))
                dve.tensor_copy(w_ext[i][:, :, 0:HF], w_raw[i][:]).then_inc(gat_ready, 1)

            def statistics(src):
                for t in range(T):
                    mark(dve.bn_stats(stats[:, t, :], src[:, t, :]))
                settle()
                for t in range(T):
                    mark(dve.bn_aggr(meanvar[:, t, :], stats[:, t, :]))
                settle()
                dve.tensor_scalar(var_eps[:], meanvar[:, :, 1], EPS, None, ALU.add).then_inc(var_ready, 1)

            def normalised(dst, src, n):
                dve.wait_ge(rstd_ready, n)
                for t in range(T):
                    ins = dve.tensor_scalar(dst[:, t, :], src[:, t, :], meanvar[:, t, 0:1],
                                            rstd[:, t:t + 1], ALU.subtract, ALU.mult)
                    if t < T - 1:
                        mark(ins)
                return ins

            def mask_stage(a):
                dve.wait_ge(x_landed, 16 * (a + 1))
                if a:
                    dve.wait_ge(mask_turned, a)
                statistics(x_in)
                link(normalised(mask, x_in, 2 * a + 1))
                link(dve.tensor_scalar(mask[:], mask[:], 1.0, MASK_SCALE, ALU.subtract, ALU.mult))
                link(dve.tensor_reduce(row_max[:], mask[:], AX.X, ALU.max))
                for t in range(T):
                    ins = dve.tensor_scalar(mask[:, t], mask[:, t], row_max[:, t:t + 1], None, ALU.subtract)
                    if t < T - 1:
                        mark(ins)
                ins.then_inc(mask_ready, 1)

            def layer_scores(a, i):
                n = LAYERS * a + i
                dve.wait_ge(rows_ready, n + 1)
                rows = ps_mix[0:2 * HEADS, 0:N]
                if n == 0:
                    dve.wait_ge(const_ready, 7)
                mark(dve.tensor_reduce(score_max[:], rows, AX.X, ALU.max))
                link(dve.tensor_copy(self_rows[0:HEADS, :], rows[0:HEADS]))
                mark(dve.tensor_tensor(self_rows[LO_ROW:LO_ROW + HEADS, :], rows[0:HEADS],
                                       self_rows[0:HEADS, :].bitcast(F32), ALU.subtract))
                dve.tensor_scalar(diag[:], ident[0:2 * HEADS, 0:2 * HEADS], score_max[:, 0:1], None,
                                  ALU.mult).then_inc(diag_ready, 1)
                dve.wait_ge(max_spread, n + 1)
                dve.tensor_copy(max_bc[:], ps_mix[:, N:N + 2 * HEADS]).then_inc(max_ready, 1)
                dve.wait_ge(max_ready, n + 1)
                dve.wait_ge(feat_ready, n + 1)
                if n:
                    dve.wait_ge(exp_done, PAIRS * n)
                mark(dve.tensor_scalar(t_08[:], t_nat[:], 1.0 - SLOPE, None, ALU.mult))
                link(dve.scalar_tensor_tensor(shift[:], max_bc[:, HEADS:], 1.0 - SLOPE, max_bc[:, 0:HEADS],
                                              ALU.mult, ALU.add))
                mark(dve.tensor_scalar(max_bc[:, 0:HEADS], max_bc[:, HEADS:], SLOPE, -HEADROOM,
                                       ALU.mult, ALU.add))
                settle()
                link(dve.scalar_tensor_tensor(shift[:], shift[:], 0.0, max_bc[:, 0:HEADS], ALU.max, ALU.add))
                dve.scalar_tensor_tensor(exp_bias[:], t_nat[:], SLOPE,
                                         shift[:].unsqueeze(1).to_broadcast([P, C, HEADS]),
                                         ALU.mult, ALU.subtract).then_inc(bias_ready, 1)

            def add_mask(a, i, p):
                n = LAYERS * a + i
                dve.wait_ge(relu_done, PAIRS * n + p + 1)
                dve.wait_ge(mask_t_ready, a + 1)
                q = prob[:, 2 * p:2 * p + 2].rearrange("p h c n -> p h (c n)")
                m = mask_t[:].rearrange("p c n -> p (c n)").unsqueeze(1).to_broadcast([P, 2, C * N])
                dve.tensor_tensor(q, q, m, ALU.add).then_inc(add_done, 1)

            def normalise(a, i):
                n = LAYERS * a + i
                dve.wait_ge(pv_done, PAIRS * (n + 1))
                if n:
                    dve.wait_ge(neg_exp, n)
                pv = [ps_row[t][:, 0:HEADS * (F_OUT + 1)].rearrange("p (h o) -> p h o", h=HEADS) for t in range(T)]
                for t in range(T):
                    mark(dve.reciprocal(inv_sum[:, t, :].unsqueeze(2), pv[t][:, :, F_OUT:F_OUT + 1]))
                settle()
                for t in range(T):
                    ins = dve.tensor_tensor(att[:, t, :].rearrange("p (h o) -> p h o", h=HEADS),
                                            pv[t][:, :, 0:F_OUT],
                                            inv_sum[:, t, :].unsqueeze(2).to_broadcast([P, HEADS, F_OUT]),
                                            ALU.mult)
                    ins.then_inc(rows_free, 1)
                dve.wait_ge(rows_free, T * (n + 1))
                link(dve.tensor_tensor(att[:], att[:], b_bc[i][:].unsqueeze(1).to_broadcast([P, T, HF]), ALU.add))
                dve.tensor_scalar(att_exp[:], att[:], 0.0, None, ALU.min).then_inc(neg_ready, 1)
                dve.wait_ge(neg_exp, n + 1)
                if i == 0:
                    if a:
                        dve.wait_ge(z_turned, a)
                    dve.scalar_tensor_tensor(att_z[:], att[:], 0.0, att_exp[:], ALU.max, ALU.add
                                             ).then_inc(z_ready, 1)
                    dve.wait_ge(z_turned, a + 1)
                    dve.tensor_scalar(h1_t[:].rearrange("p c n -> p (c n)"), ps_mix[:], 1.0, None,
                                      ALU.subtract).then_inc(h1_ready, 1)
                else:
                    link(dve.scalar_tensor_tensor(att[:], att[:], 0.0, att_exp[:], ALU.max, ALU.add))
                    dve.wait_ge(xg_ready, a + 1)
                    if a:
                        dve.wait_ge(x2_moved, a)
                    dve.scalar_tensor_tensor(x2[:], att[:], gate[:, 0:1], x_less_gate[:],
                                             ALU.mult, ALU.add).then_inc(x2_ready, 1)

            def hat(a):
                dve.wait_ge(x2_ready, a + 1)
                statistics(x2)
                if a:
                    dve.wait_ge(xhat_turned, a)
                normalised(x_hat, x2, 2 * a + 2).then_inc(xhat_ready, 1)
                dve.wait_ge(stage_hi_ready, a + 1)
                if a:
                    dve.wait_ge(x_lo_moved, a)
                dve.tensor_tensor(stage_lo[:].rearrange("p c n -> p (c n)"), ps_mix[:],
                                  stage_hi[:].rearrange("p c n -> p (c n)").bitcast(F32),
                                  ALU.subtract).then_inc(stage_ready, 1)

            def top_two(a):
                logits = ps_mix[:, 0:T * EXPERTS].rearrange("p (t e) -> p t e", t=T)
                dve.wait_ge(logits_ready, a + 1)
                if a:
                    dve.wait_ge(comb_turned, a)
                mark(dve.tensor_reduce(logit_max[:], logits, AX.X, ALU.max))
                link(dve.tensor_tensor(biased[:], logits, rbias[:].unsqueeze(1).to_broadcast([P, T, EXPERTS]),
                                       ALU.add))
                dve.tensor_tensor(r_exp[:], logits, logit_max[:].unsqueeze(2).to_broadcast([P, T, EXPERTS]),
                                  ALU.subtract).then_inc(rexp_in, 1)
                for t in range(T):
                    mark(dve.max(top8[:, t], biased[:, t]))
                settle()
                for t in range(T):
                    mark(dve.max_index(top_at[:, t], top8[:, t], biased[:, t]))
                settle()
                link(dve.tensor_copy(top_at_f[:], top_at[:]))
                for t in range(T):
                    mark(dve.tensor_scalar(picked[:, t], expert_id[:], top_at_f[:, t, 0:1], None, ALU.is_equal))
                settle()
                for t in range(T):
                    mark(dve.scalar_tensor_tensor(picked[:, t], expert_id[:], top_at_f[:, t, 1:2], picked[:, t],
                                                  ALU.is_equal, ALU.add))
                settle()
                dve.wait_ge(rexp_out, a + 1)
                link(dve.tensor_tensor(picked[:], picked[:], r_exp[:], ALU.mult))
                link(dve.tensor_reduce(r_sum[:], picked[:], AX.X, ALU.add))
                link(dve.reciprocal(r_inv[:], r_sum[:]))
                dve.scalar_tensor_tensor(combine[:], picked[:], 0.5,
                                         r_inv[:].unsqueeze(2).to_broadcast([P, T, EXPERTS]),
                                         ALU.mult, ALU.mult).then_inc(comb_ready, 1)

            def combine_rows(a):
                dve.wait_ge(comb_turned, a + 1)
                if a:
                    dve.wait_ge(comb_spread, EXPERTS // 2 * a)
                rows = ps_mix[0:EXPERTS, 0:N]
                link(dve.tensor_copy(comb_rows[0:EXPERTS, :], rows))
                dve.tensor_tensor(comb_rows[LO_ROW:LO_ROW + EXPERTS, :], rows,
                                  comb_rows[0:EXPERTS, :].bitcast(F32), ALU.subtract
                                  ).then_inc(comb_rows_ready, 1)

            def attention(a, s):
                if s == MASK:
                    mask_stage(a)
                for i in range(LAYERS):
                    if s == LAYER_AT[i]:
                        layer_scores(a, i)
                    p = s - LAYER_AT[i] - 1
                    if 0 <= p < PAIRS:
                        add_mask(a, i, p)
                    if s == NORM_AT[i]:
                        normalise(a, i)
                if s == HAT_AT:
                    hat(a)
                if s == TOP_AT:
                    top_two(a)
                if s == COMB_AT:
                    combine_rows(a)

            def step(g, e):
                n = STEPS * g + e
                u, gt = ps_ug[e % UG_BANKS][:, 0, :], ps_ug[e % UG_BANKS][:, 1, :]
                dve.wait_ge(tanh_done, n + 1)
                dve.scalar_tensor_tensor(hid[:, e % 2], th[:, e % 2], 1.0, u, ALU.add, ALU.mult
                                         ).then_inc(dve_ffn, 1)
                marks[1] += 1
                dve.wait_ge(dve_ffn, marks[1])
                if n >= 3:
                    dve.wait_ge(down_done, n - 2)
                if e < EXPERTS:
                    dve.tensor_tensor(hid[:, e % 2], hid[:, e % 2], gt, ALU.mult).then_inc(ug_read, 1)
                    dve.wait_ge(ug_read, n + 1)
                    dve.wait_ge(comb_spread, EXPERTS // 2 * g + e // 2 + 1)
                    dve.tensor_tensor(hid_out[:, e % 3], hid[:, e % 2], ps_comb[:, e % 2, :], ALU.mult
                                      ).then_inc(hid_ready, 1)
                else:
                    dve.scalar_tensor_tensor(hid_out[:, e % 3], hid[:, e % 2], 0.5, gt, ALU.mult, ALU.mult
                                             ).then_inc(ug_read, 1)

            def final(g):
                dve.wait_ge(down_done, STEPS * (g + 1))
                dve.wait_ge(x2_moved, g + 1)
                if g:
                    dve.wait_ge(out_stored, 16 * g)
                dve.scalar_tensor_tensor(y_out[:], ps_acc[:], gate[:, 1:2], x2_ffn[:], ALU.mult, ALU.add
                                         ).then_inc(y_ready, 1)

            def move_lo(g):
                dve.wait_ge(stage_ready, g + 1)
                if g:
                    dve.wait_ge(up_done, STEPS * g)
                dve.tensor_copy(x_lo[:], stage_lo[:].bitcast(F32)).then_inc(x_lo_moved, 1)

            dve.wait_ge(gate_ready, 1)
            mask_stage(0)
            gat_weights(0)
            gat_weights(1)
            for s in range(1, 4):
                attention(0, s)
            dve.wait_ge(router_landed, 32)
            link(dve.tensor_copy(rt_hi[:], rt_raw[:]))
            dve.tensor_tensor(rt_lo[:], rt_raw[:], rt_hi[:].bitcast(F32), ALU.subtract).then_inc(rt_ready, 1)
            for s in range(4, STEPS):
                attention(0, s)
            for g in range(B):
                move_lo(g)
                for e in range(STEPS):
                    step(g, e)
                    if g + 1 < B:
                        attention(g + 1, e)
                final(g)

        @block.tensor
        def _(pe):
            def turn_mask(a):
                pe.wait_ge(mask_ready, a + 1)
                if a:
                    pe.wait_ge(comb_rows_ready, a)
                for t in range(T):
                    for c in range(C):
                        last = pe.transpose(ps_mix[:, c * N + t * P:c * N + (t + 1) * P],
                                            mask[:, t, c * P:(c + 1) * P], ident[:])
                last.then_inc(mask_turned, 1)

            def layer(a, i):
                n = LAYERS * a + i
                pe.wait_ge(gat_ready, i + 1)
                if i == 0:
                    pe.wait_ge(ctx_landed, 16 * (a + 1))
                    pe.wait_ge(mask_t_ready, a + 1)
                else:
                    pe.wait_ge(h1_ready, a + 1)
                src = xc_t if i == 0 else h1_t
                chunks = src.shape[1]
                for c in range(chunks):
                    last = pe.matmul(ps_mix[0:2 * HEADS, 0:N], w_score[i][:, c, :], src[:, c, :],
                                     start=(c == 0), stop=(c == chunks - 1))
                last.then_inc(rows_ready, 1)
                if n:
                    pe.wait_ge(rows_free, T * n)
                for t in range(T):
                    for c in range(chunks):
                        last = pe.matmul(ps_row[t][:, 0:WE], src[:, c, t * P:(t + 1) * P], w_ext[i][:, c, :],
                                         start=(c == 0), stop=(c == chunks - 1))
                last.then_inc(feat_ps, 1)
                pe.wait_ge(diag_ready, n + 1)
                pe.matmul(ps_mix[:, N:N + 2 * HEADS], ones[:], diag[:], start=True, stop=True
                          ).then_inc(max_spread, 1)

            def spread_self(a, i, p):
                n = LAYERS * a + i
                if p == 0:
                    pe.wait_ge(max_ready, n + 1)
                else:
                    pe.wait_ge(relu_done, PAIRS * n + p)
                if n == 0 and p == 0:
                    pe.wait_ge(sel_ready, 1)
                for k in range(2):
                    last = pe.matmul(mix_pair[:, k, :], sel[:, 2 * p + k, :], self_rows[:], start=True, stop=True)
                last.then_inc(self_spread, 1)

            def weighted(a, i, p):
                n = LAYERS * a + i
                pe.wait_ge(exp_done, PAIRS * n + p + 1)
                if p == 0:
                    pe.wait_ge(feat_ready, n + 1)
                for h in range(2 * p, 2 * p + 2):
                    for t in range(T):
                        for c in range(C):
                            last = pe.matmul(ps_row[t][:, h * (F_OUT + 1):(h + 1) * (F_OUT + 1)],
                                             prob[:, h, c, t * P:(t + 1) * P], feat[:, c, h, :],
                                             start=(c == 0), stop=(c == C - 1))
                last.then_inc(pv_done, 1)

            def turn_rows(src, ready, done, a, free=None):
                pe.wait_ge(ready, a + 1)
                if free is not None:
                    pe.wait_ge(*free)
                for t in range(T):
                    for c in range(C):
                        last = pe.transpose(ps_mix[:, c * N + t * P:c * N + (t + 1) * P],
                                            src[:, t, c * P:(c + 1) * P], ident[:])
                last.then_inc(done, 1)

            def route(a):
                pe.wait_ge(stage_ready, a + 1)
                if a == 0:
                    pe.wait_ge(rt_ready, 1)
                for t in range(T):
                    parts = [(stage_hi, rt_hi), (stage_lo, rt_hi), (stage_hi, rt_lo)]
                    todo = [(c, l, r) for c in range(C) for l, r in parts]
                    for k, (c, l, r) in enumerate(todo):
                        last = pe.matmul(ps_mix[:, t * EXPERTS:(t + 1) * EXPERTS], l[:, c, t * P:(t + 1) * P],
                                         r[:, c, :], start=(k == 0), stop=(k == len(todo) - 1))
                last.then_inc(logits_ready, 1)

            def turn_combine(a):
                pe.wait_ge(comb_ready, a + 1)
                for t in range(T):
                    last = pe.transpose(ps_mix[0:EXPERTS, t * P:(t + 1) * P], combine[:, t, :], ident[:])
                last.then_inc(comb_turned, 1)

            def attention(a, s):
                if s == MASK_T:
                    turn_mask(a)
                for i in range(LAYERS):
                    if s == LAYER_AT[i]:
                        layer(a, i)
                    p = s - LAYER_AT[i] - 1
                    if 0 <= p < PAIRS:
                        spread_self(a, i, p)
                    if 0 <= p - 1 < PAIRS:
                        weighted(a, i, p - 1)
                if s == NORM_AT[0]:
                    turn_rows(att_z, z_ready, z_turned, a, (relu_done, PAIRS * (LAYERS * a + 1)))
                if s == HAT_AT:
                    turn_rows(x_hat, xhat_ready, xhat_turned, a, (relu_done, PAIRS * (LAYERS * a + 2)))
                if s == ROUTE_AT:
                    route(a)
                if s == COMB_AT:
                    turn_combine(a)

            def up(g, e):
                n = STEPS * g + e
                if e == 0:
                    pe.wait_ge(x_hi_moved, g + 1)
                    pe.wait_ge(x_lo_moved, g + 1)
                if g == 0:
                    pe.wait_ge(up_ready, e + 1)
                if n >= UG_BANKS:
                    pe.wait_ge(ug_read, n - UG_BANKS + 1)
                for k in range(2):
                    parts = [(up_hi, x_hi), (up_hi, x_lo), (up_lo, x_hi)]
                    todo = [(c, w, m) for c in range(C) for w, m in parts]
                    for j, (c, w, m) in enumerate(todo):
                        last = pe.matmul(ps_ug[e % UG_BANKS][:, k, :], w[:, e, k, c * P:(c + 1) * P],
                                         m[:, c, :], start=(j == 0), stop=(j == len(todo) - 1))
                last.then_inc(up_done, 1)

            def spread_combine(g, e):
                if e == 0:
                    pe.wait_ge(comb_rows_ready, g + 1)
                if n_routed(g, e):
                    pe.wait_ge(hid_ready, n_routed(g, e))
                for k in range(2):
                    last = pe.matmul(ps_comb[:, k, :], sel[:, e + k, :], comb_rows[:], start=True, stop=True)
                last.then_inc(comb_spread, 1)

            def n_routed(g, e):
                return EXPERTS * g + e

            def down(g, e):
                n = STEPS * g + e
                if e < EXPERTS:
                    pe.wait_ge(hid_ready, EXPERTS * g + e + 1)
                else:
                    pe.wait_ge(ug_read, n + 1)
                if e == 0:
                    if g:
                        pe.wait_ge(y_ready, g)
                    else:
                        pe.wait_ge(down_landed, 32)
                for t in range(T):
                    last = pe.matmul(ps_acc[:, t, :], hid_out[:, e % 3, t * P:(t + 1) * P], down_w[:, e, :],
                                     start=(e == 0 and t == 0), stop=(e == STEPS - 1), skip_group_check=True)
                last.then_inc(down_done, 1)

            pe.wait_ge(const_ready, 7)
            for s in range(STEPS):
                attention(0, s)
            for g in range(B):
                for e in range(STEPS):
                    if e % 2 == 0 and e < EXPERTS:
                        spread_combine(g, e)
                    up(g, e)
                    if e >= LAG:
                        down(g, e - LAG)
                    if g + 1 < B:
                        attention(g + 1, e)
                for e in range(STEPS - LAG, STEPS):
                    down(g, e)


def kernel(**inputs):
    import numpy as _np
    import concourse.bacc as _bacc
    from concourse import mybir as _mybir
    from concourse.bass_utils import run_bass_kernel_spmd as _run

    a = {k: _np.asarray(v) for k, v in inputs.items()}
    p = P

    def by_row_chunk(w):
        e, d, f = w.shape
        return w.reshape(e, d // p, p, f).transpose(2, 0, 1, 3).reshape(p, e, (d // p) * f)

    def shared_up(w):
        return by_row_chunk(w[0].reshape(w.shape[1], -1, p).transpose(1, 0, 2))

    heads_last = {k: a[k].transpose(1, 0, 2).reshape(a[k].shape[1], -1) for k in ("L0_xattn_W0", "L0_xattn_W1")}
    laid = {
        "x": a["x"],
        "ctx_t": a["ctx_512"].transpose(0, 2, 1),
        "gates": _np.concatenate([a["g_xattn"].reshape(-1), a["g_ffn"].reshape(-1)]),
        "w0": heads_last["L0_xattn_W0"],
        "w1": heads_last["L0_xattn_W1"],
        "a_self": _np.stack([a["L0_xattn_a_self0"].reshape(-1), a["L0_xattn_a_self1"].reshape(-1)]),
        "a_neigh": _np.stack([a["L0_xattn_a_neigh0"].reshape(-1), a["L0_xattn_a_neigh1"].reshape(-1)]),
        "b0": a["L0_xattn_b0"].reshape(-1),
        "b1": a["L0_xattn_b1"].reshape(-1),
        "router_t": a["L0_ffn_router_w"].T,
        "router_bias": a["L0_ffn_router_bias"],
        "wu": by_row_chunk(a["L0_ffn_Wu"]),
        "wg": by_row_chunk(a["L0_ffn_Wg"]),
        "su": shared_up(a["L0_ffn_Su"]),
        "sg": shared_up(a["L0_ffn_Sg"]),
        "wd": a["L0_ffn_Wd"].transpose(1, 0, 2),
        "sd": a["L0_ffn_Sd"][0].reshape(-1, p, a["x"].shape[2]).transpose(1, 0, 2),
    }
    nc = _bacc.Bacc("TRN2", target_bir_lowering=False, num_devices=1)
    arrays, args = {}, []
    for name, v in laid.items():
        v = _np.ascontiguousarray(v)
        arrays[f"in_{name}"] = v
        args.append(nc.dram_tensor(f"in_{name}", v.shape, _mybir.dt.from_np(v.dtype), kind="ExternalInput").ap())
    args.append(nc.dram_tensor("out", a["x"].shape, _mybir.dt.from_np(a["x"].dtype), kind="ExternalOutput").ap())
    flamingo_block(nc, *args)
    return _run(nc, [arrays], core_ids=[0]).results[0]["out"]
```
